# Optimizing a Trainium2 kernel written in Bass

```python
import numpy as np
import jax
import jax.numpy as jnp

def _softmax(x, axis=-1):
    return jax.nn.softmax(x, axis=axis)

def _gelu(x):
    return jax.nn.gelu(x, approximate=True)

def _silu(x):
    return jax.nn.silu(x)

def _sigmoid(x):
    return jax.nn.sigmoid(x)

def _layernorm(x, axis=-1, eps=1e-05):
    m = jnp.mean(x, axis=axis, keepdims=True)
    v = jnp.var(x, axis=axis, keepdims=True)
    return (x - m) / jnp.sqrt(v + eps)

def _scatter_add(tgt, idx, src, axis=0):
    return tgt.at[idx].add(src)

def _segment_sum(src, seg, n):
    return jax.ops.segment_sum(src, seg, n)
kernel_name = 'mk_adaln_ffn_d1_seqx_r4_cbbf86'

def setup_inputs(seed: int=0):
    np.random.seed(seed)
    _w = jnp.asarray

    def _rec_inputs():
        import jax
        import jax.numpy as jnp
        _rk = jax.random.key(seed)
        x = -7.109e-05 + 0.9999 * jax.random.normal(jax.random.fold_in(_rk, 1), (64, 64, 1024), jnp.float32)
        _lenS = 64 - jax.random.randint(jax.random.fold_in(_rk, 7), (64,), 0, max(1, 64 // 4) + 1, jnp.int32)
        _lenS2 = 64 - jax.random.randint(jax.random.fold_in(_rk, 8), (64,), 0, max(1, 64 // 4) + 1, jnp.int32)
        itok_B_0_15 = jax.random.randint(jax.random.fold_in(_rk, 11), (64,), 0, 16, jnp.int32)
        return (x, itok_B_0_15)
    x, itok_B_0_15 = _rec_inputs()

    def _L0_cond_setup():
        import jax, jax.numpy as jnp
        import numpy as np
        B, C, T = (64, 64, 1024)
        S, D = (16, 64)
        key = jax.random.key(seed)
        k1, k2, k3 = jax.random.split(key, 3)
        x = jax.random.normal(k1, (B, C, T), dtype=jnp.float32)
        condition = jax.random.randint(k2, (B,), 0, S, dtype=jnp.int64)
        bound = float(np.sqrt(6.0 / C))
        weights = jax.random.uniform(k3, (S, C, D), dtype=jnp.float32, minval=-bound, maxval=bound)
        return {'x': x, 'condition': condition, 'weights': weights}
    _L0_cond_all = _L0_cond_setup()
    _L0_cond_in = {k: v for k, v in _L0_cond_all.items() if k in ('weights',)}
    del _L0_cond_all

    def _L0_ffn_setup():
        import jax, jax.numpy as jnp
        import numpy as np
        NUM_EXPERTS = 4
        HIDDEN = 1024
        RANK = 8
        ALPHA = 8.0
        SCALE = ALPHA / RANK
        key = jax.random.key(seed)
        ks = jax.random.split(key, 6)
        B, T, H, E, R = (4, 1024, HIDDEN, NUM_EXPERTS, RANK)
        x = jax.random.normal(ks[0], (B, T, H), dtype=jnp.float32)
        W_up = jax.random.normal(ks[1], (H, H), dtype=jnp.float32) / np.sqrt(H)
        gate_w = jax.random.normal(ks[2], (E, H), dtype=jnp.float32) / np.sqrt(H)
        expert_bias = jnp.zeros((E,), dtype=jnp.float32)
        lora_A = jax.random.normal(ks[3], (E, R, H), dtype=jnp.float32) / np.sqrt(H)
        lora_B = jax.random.normal(ks[4], (E, H, R), dtype=jnp.float32) * 0.01
        return {'x': x, 'W_up': W_up, 'gate_w': gate_w, 'expert_bias': expert_bias, 'lora_A': lora_A, 'lora_B': lora_B}
    _L0_ffn_all = _L0_ffn_setup()
    _L0_ffn_in = {k: v for k, v in _L0_ffn_all.items() if k in ('W_up', 'gate_w', 'expert_bias', 'lora_A', 'lora_B')}
    del _L0_ffn_all
    return {'x': x, 'itok_B_0_15': itok_B_0_15, 'L0_cond_weights': _L0_cond_in['weights'], 'L0_ffn_W_up': _L0_ffn_in['W_up'], 'L0_ffn_gate_w': _L0_ffn_in['gate_w'], 'L0_ffn_expert_bias': _L0_ffn_in['expert_bias'], 'L0_ffn_lora_A': _L0_ffn_in['lora_A'], 'L0_ffn_lora_B': _L0_ffn_in['lora_B']}

def reference(x, itok_B_0_15, L0_cond_weights, L0_ffn_W_up, L0_ffn_gate_w, L0_ffn_expert_bias, L0_ffn_lora_A, L0_ffn_lora_B):
    import jax
    import jax.numpy as jnp

    def _L0_cond_ref(x, condition, weights):
        import jax, jax.numpy as jnp
        import numpy as np
        B, C, T = (64, 64, 1024)
        S, D = (16, 64)
        W = weights[condition]
        return jnp.einsum('bct,bcd->bdt', x, W)

    def _L0_ffn_ref(x, W_up, gate_w, expert_bias, lora_A, lora_B):
        import jax, jax.numpy as jnp
        import numpy as np
        NUM_EXPERTS = 4
        HIDDEN = 1024
        RANK = 8
        ALPHA = 8.0
        SCALE = ALPHA / RANK
        B, T, H = x.shape
        E = gate_w.shape[0]
        x_flat = x.reshape(-1, H)
        logits = x_flat @ gate_w.T + expert_bias
        top1 = jnp.argmax(logits, axis=-1)
        one_hot = jax.nn.one_hot(top1, E, dtype=x_flat.dtype)
        base_out = jnp.einsum('bth,oh->bto', x, W_up)
        z = jnp.einsum('nh,erh->ner', x_flat, lora_A)
        d = jnp.einsum('ner,ehr->neh', z, lora_B) * SCALE
        delta = jnp.einsum('neh,ne->nh', d, one_hot)
        return base_out + delta.reshape(B, T, H)
    x = x + _L0_ffn_ref(_L0_cond_ref(x, itok_B_0_15, L0_cond_weights), L0_ffn_W_up, L0_ffn_gate_w, L0_ffn_expert_bias, L0_ffn_lora_A, L0_ffn_lora_B)
    return x

_drawn_inputs = setup_inputs


def setup_inputs(seed=0):
    import zlib

    import numpy as np

    out = dict(_drawn_inputs(seed))
    spreads = {'L0_ffn_expert_bias': (0.0, 0.1)}
    factors = {}
    for name, (base, spread) in spreads.items():
        noise = np.random.default_rng([zlib.crc32(name.encode()), seed]).standard_normal(out[name].shape)
        drawn = base * np.exp(spread * noise) if base else spread * noise
        out[name] = jnp.asarray(drawn.astype(out[name].dtype))
    for name, factor in factors.items():
        out[name] = (out[name] * factor).astype(out[name].dtype)
    return out
```

```python
import concourse.bass as bass
from concourse import mybir
from contextlib import ExitStack


def adaln_ffn_kernel(
    nc: bass.Bass,
    x: bass.AP,
    cond_index: bass.AP,
    cond_weights: bass.AP,
    w_up: bass.AP,
    gate_w: bass.AP,
    expert_bias: bass.AP,
    lora_a: bass.AP,
    lora_b: bass.AP,
    out: bass.AP,
):
    fp32 = mybir.dt.float32
    fp32r = mybir.dt.float32r
    i32 = mybir.dt.int32
    ALU = mybir.AluOpType
    ACT = mybir.ActivationFunctionType
    AX = mybir.AxisListType

    B, C, T = x.shape
    S, _, D = cond_weights.shape
    O, _ = w_up.shape
    E, R, _ = lora_a.shape
    P = 128
    PAIRS = B // 2
    KC = T // P
    OC = O // P
    HALF = 512
    HALVES = O // HALF
    OCH = OC // HALVES
    ER = E * R
    GC = E + ER
    UNROLL = 4
    YB = 2
    KB = KC // YB
    ROUTE_STEPS = 8
    assert C == D and 2 * D == P and PAIRS % UNROLL == 0 and PAIRS > 2 * UNROLL

    x_pairs = x.rearrange("(n b) c t -> n (b c) t", b=2)
    out_pairs = out.rearrange("(n b) c t -> n (b c) t", b=2)

    ctx = ExitStack()
    with ctx:
        def sb(name, shape, dt):
            return ctx.enter_context(nc.sbuf_tensor(name, shape, dt))

        def bank(name):
            return ctx.enter_context(nc.psum_tensor(name, [P, HALF], fp32))

        def sem(name):
            return ctx.enter_context(nc.semaphore(name))

        w_up_sb = sb("w_up_sb", [P, OC, T], fp32)
        cond_sb = sb("cond_sb", [P, S, D], fp32)
        router_sb = sb("router_sb", [GC, T], fp32)
        lora_b_sb = sb("lora_b_sb", [P, E, OC, R], fp32)
        bias_sb = sb("bias_sb", [P, GC], fp32)
        index_sb = sb("index_sb", [1, B], i32)
        wh = sb("wh", [P, KC, O], fp32r)
        wl = sb("wl", [P, KC, O], fp32r)
        cond_hl = sb("cond_hl", [P, S, 2, D], fp32r)
        router_hl = sb("router_hl", [P, KC, 2, GC], fp32r)
        lora_b4 = sb("lora_b4", [P, OC, 4, ER], fp32)
        lora_b_hl = sb("lora_b_hl", [P, O], fp32r)
        ident = sb("ident", [P, P], fp32)
        rank_w = sb("rank_w", [P, E], fp32)
        x_sb = sb("x_sb", [P, UNROLL, T], fp32)
        x_hl = sb("x_hl", [P, 2, 2, T], fp32r)
        yh = sb("yh", [P, 2, KC, P], fp32r)
        yl = sb("yl", [P, 2, KC, P], fp32r)
        out_sb = sb("out_sb", [P, 2, O], fp32)
        low_sum = sb("low_sum", [P, GC], fp32)
        scores = sb("scores", [P, GC], fp32)
        best = sb("best", [P, 1], fp32)
        ranks = sb("ranks", [P, E], fp32)
        first = sb("first", [P, 1], fp32)
        z_sel = sb("z_sel", [P, ER], fp32)
        z_parts = sb("z_parts", [P, 4, ER], fp32)
        z_t = sb("z_t", [P, 2, P], fp32r)

        out_ps = [[bank(f"out_ps{s}{h}") for h in range(HALVES)] for s in range(2)]
        y_ps = [bank(f"y_ps{n}") for n in range(YB)]
        score_ps = bank("score_ps")
        z_ps = bank("z_ps")

        ident_zero = sem("ident_zero")
        ident_done = sem("ident_done")
        const_done = sem("const_done")
        bias_zero = sem("bias_zero")
        cond_loaded = sem("cond_loaded")
        index_loaded = sem("index_loaded")
        router_loaded = sem("router_loaded")
        bias_loaded = sem("bias_loaded")
        lora_b_loaded = sem("lora_b_loaded")
        w_up_loaded = [sem(f"w_up_loaded{h}") for h in range(HALVES)]
        x_loaded = [sem(f"x_loaded{s}") for s in range(UNROLL)]
        stored = [sem(f"stored{s}") for s in range(2)]
        cond_high = sem("cond_high")
        cond_low = sem("cond_low")
        router_t = sem("router_t")
        router_high = sem("router_high")
        router_low = sem("router_low")
        lora_b_copied = sem("lora_b_copied")
        lora_b_t = sem("lora_b_t")
        lora_b_high = sem("lora_b_high")
        lora_b_low = sem("lora_b_low")
        w_t = sem("w_t")
        w_high = sem("w_high")
        w_low = sem("w_low")
        x_high = sem("x_high")
        x_low = sem("x_low")
        y_done = sem("y_done")
        y_high = sem("y_high")
        y_low = sem("y_low")
        scored = sem("scored")
        route_step = sem("route_step")
        z_turned = sem("z_turned")
        z_ready = sem("z_ready")
        half_done = sem("half_done")
        half_out = sem("half_out")

        block = ctx.enter_context(nc.Block())

        def in_groups(eng, work):
            for n in range(UNROLL):
                work(n, n, True, False)
            with eng.Fori(1, PAIRS // UNROLL - 1) as group:
                for n in range(UNROLL):
                    work(group * UNROLL + n, n, False, False)
            for n in range(UNROLL):
                work(PAIRS - UNROLL + n, n, False, True)

        @block.sync
        def _(sp):
            sp.dma_start(x_sb[:, 0, :], x_pairs[0]).then_inc(x_loaded[0], 16)
            for h in range(HALVES):
                sp.dma_start(w_up_sb[:, h * OCH:(h + 1) * OCH, :],
                             w_up[h * HALF:(h + 1) * HALF, :].rearrange("(c p) t -> p c t", p=P))\
                  .then_inc(w_up_loaded[h], 16)
            for s in range(1, UNROLL):
                sp.dma_start(x_sb[:, s, :], x_pairs[s]).then_inc(x_loaded[s], 16)

            def turn(p, s, opening, closing):
                sp.wait_ge(half_out, HALVES * p + HALVES)
                sp.dma_start(out_pairs[p], out_sb[:, s % 2, :]).then_inc(stored[s % 2], 16)
                if not closing:
                    sp.dma_start(x_sb[:, s, :], x_pairs[p + UNROLL]).then_inc(x_loaded[s], 16)

            in_groups(sp, turn)
            for s in range(2):
                sp.wait_ge(stored[s], 16 * (PAIRS // 2))

        @block.gpsimd
        def _(pool):
            pool.memset(ident[:, :], 0.0).then_inc(ident_zero, 1)
            pool.memset(bias_sb[:, :], 0.0).then_inc(bias_zero, 1)
            pool.wait_ge(ident_zero, 1)
            pool.affine_select(out=ident[:, :], in_=ident[:, :], compare_op=ALU.not_equal, fill=1.0,
                               base=0, pattern=[[-1, P]], channel_multiplier=1).then_inc(ident_done, 1)
            for e in range(E):
                pool.memset(rank_w[:, e:e + 1], float(E - e)).then_inc(const_done, 1)

        @block.scalar
        def _(act):
            src = cond_weights.rearrange("s c d -> c s d")
            for part in range(2):
                act.dma_start(cond_sb[part * C:(part + 1) * C, :, :], src).then_inc(cond_loaded, 16)
            act.dma_start(index_sb[:, :], cond_index.rearrange("(a n) -> a n", a=1)).then_inc(index_loaded, 16)
            act.dma_start(router_sb[0:E, :], gate_w).then_inc(router_loaded, 16)
            act.dma_start(router_sb[E:GC, :], lora_a.rearrange("e r t -> (e r) t")).then_inc(router_loaded, 16)
            act.dma_start(lora_b_sb[:, :, :, :], lora_b.rearrange("e (p j) r -> p e j r", p=P))\
               .then_inc(lora_b_loaded, 16)
            act.wait_ge(bias_zero, 1)
            act.dma_start(bias_sb[:, 0:E], expert_bias.rearrange("(a n) -> a n", a=1).to_broadcast([P, E]))\
               .then_inc(bias_loaded, 16)

            def split_x(p, s, opening):
                act.wait_ge(x_loaded[s], 16 // UNROLL * (p - s) + 16)
                if not opening or p >= 2:
                    act.wait_ge(y_done, YB * p - YB)
                for b in range(2):
                    rows = slice(b * C, (b + 1) * C)
                    act.activation(x_hl[rows, s % 2, b, :], x_sb[rows, s, :], ACT.Copy).then_inc(x_high, 1)

            def split_y(p, s, opening):
                for n in range(YB):
                    act.wait_ge(y_done, YB * p + n + 1)
                    if n == 0 and (not opening or p >= 2):
                        act.wait_ge(half_done, HALVES * p - HALVES)
                    act.activation(yh[:, s % 2, n * KB:(n + 1) * KB, :], y_ps[n][:, :], ACT.Copy).then_inc(y_high, 1)

            def split_w(h):
                for k in range(KC):
                    n = h * KC + k
                    act.wait_ge(w_t, n + 1)
                    act.activation(wh[:, k, h * HALF:(h + 1) * HALF], out_ps[1][n % 2][:, :], ACT.Copy)\
                       .then_inc(w_high, 1)

            split_x(0, 0, True)
            act.wait_ge(cond_loaded, 32)
            act.activation(cond_hl[:, :, 0, :], cond_sb[:, :, :], ACT.Copy).then_inc(cond_high, 1)
            act.wait_ge(router_t, 1)
            act.activation(router_hl[:, :, 0, :], score_ps[:, 0:KC * GC], ACT.Copy).then_inc(router_high, 1)
            act.wait_ge(lora_b_t, 1)
            for n in range(2):
                j = OC // 2
                act.activation(lora_b_hl[:, :].rearrange("q (p j) -> q j p", j=OC)[:, n * j:(n + 1) * j, :],
                               out_ps[0][n][:, :].rearrange("q (j p) -> q j p", j=j),
                               ACT.Copy).then_inc(lora_b_high, 1)
            split_x(1, 1, True)
            split_y(0, 0, True)
            split_w(0)

            def turn(p, s, opening, closing):
                if opening and s == 0:
                    split_w(1)
                if not closing or s + 2 < UNROLL:
                    split_x(p + 2, (s + 2) % UNROLL, opening)
                act.wait_ge(z_turned, p + 1)
                if not opening or p >= 2:
                    act.wait_ge(half_done, HALVES * p - HALVES)
                act.activation(z_t[:, s % 2, :], z_ps[:, 0:P], ACT.Copy).then_inc(z_ready, 1)
                if not closing or s + 1 < UNROLL:
                    split_y(p + 1, (s + 1) % UNROLL, opening)

            in_groups(act, turn)

        @block.tensor
        def _(pe):
            def load_index(p):
                return [pe.value_load(index_sb[0:1, bass.ds(2 * p + b, 1)], min_val=0, max_val=S - 1)
                        for b in range(2)]

            def make_y(p, s, opening, index):
                pe.wait_ge(x_low, 2 * p + 2)
                if not opening or p >= 1:
                    pe.wait_ge(y_low, YB * p)
                for n in range(YB):
                    for k in range(n * KB, (n + 1) * KB):
                        for b in range(2):
                            at = (k - n * KB) * P + b * D
                            for part in range(2):
                                mm = pe.matmul(y_ps[n][:, at:at + D], x_hl[:, s % 2, b, k * P:(k + 1) * P],
                                               cond_hl[:, index[b], part, :], start=(part == 0), stop=(part == 1))
                    mm.then_inc(y_done, 1)

            def turn_w(h):
                pe.wait_ge(w_up_loaded[h], 16)
                for k in range(KC):
                    n = h * KC + k
                    if n >= 2:
                        pe.wait_ge(w_low, n - 1)
                    for c in range(OCH):
                        mm = pe.transpose(out_ps[1][n % 2][:, c * P:(c + 1) * P],
                                          w_up_sb[:, h * OCH + c, k * P:(k + 1) * P], ident[:, :])
                    mm.then_inc(w_t, 1)

            pe.wait_ge(ident_done, 1)
            pe.wait_ge(router_loaded, 32)
            for k in range(KC):
                mm = pe.transpose(score_ps[:, k * GC:(k + 1) * GC], router_sb[:, k * P:(k + 1) * P],
                                  ident[0:GC, 0:GC])
            mm.then_inc(router_t, 1)
            pe.wait_ge(lora_b_copied, 1)
            for j in range(OC):
                mm = pe.transpose(out_ps[0][j * 2 // OC][:, j % (OC // 2) * P:(j % (OC // 2) + 1) * P],
                                  lora_b4[:, j, :, :].rearrange("p n q -> p (n q)"), ident[:, :])
            mm.then_inc(lora_b_t, 1)
            pe.wait_ge(index_loaded, 16)
            pe.wait_ge(cond_low, 1)
            make_y(0, 0, True, load_index(0))
            turn_w(0)

            def turn(p, s, opening, closing):
                last = closing and s + 1 == UNROLL
                index = None if last else load_index(p + 1)
                pe.wait_ge(y_low, YB * p + YB)
                if opening and p == 0:
                    pe.wait_ge(router_low, 1)
                else:
                    pe.wait_ge(route_step, ROUTE_STEPS * p)
                for k in range(KC):
                    for part, y in enumerate((yh, yl)):
                        mm = pe.matmul(score_ps[:, 0:2 * GC], y[:, s % 2, k, :],
                                       router_hl[:, k, :, :], start=(k == 0 and part == 0),
                                       stop=(k == KC - 1 and part == 1))
                mm.then_inc(scored, 1)

                def base(h):
                    if opening and p == 0:
                        pe.wait_ge(w_low, (h + 1) * KC)
                        if h == 0:
                            pe.wait_ge(lora_b_low, 2)
                    if not opening or p >= 2:
                        pe.wait_ge(half_out, HALVES * (p - 2) + h + 1)
                    cols = slice(h * HALF, (h + 1) * HALF)
                    for k in range(KC):
                        for y, w in ((yh, wh), (yh, wl), (yl, wh)):
                            pe.matmul(out_ps[s % 2][h][:, :], y[:, s % 2, k, :], w[:, k, cols],
                                      start=(k == 0 and w is wh and y is yh), stop=False)

                base(0)
                if opening and s == 0:
                    turn_w(1)
                pe.wait_ge(route_step, ROUTE_STEPS * p + ROUTE_STEPS)
                if not opening or p >= 1:
                    pe.wait_ge(z_ready, p)
                pe.transpose(z_ps[:, 0:P], z_parts[:, :, :].rearrange("p n q -> p (n q)"), ident[:, :])\
                  .then_inc(z_turned, 1)
                if not last:
                    make_y(p + 1, (s + 1) % UNROLL, opening, index)
                base(1)
                pe.wait_ge(z_ready, p + 1)
                for h in range(HALVES):
                    pe.matmul(out_ps[s % 2][h][:, :], z_t[:, s % 2, :], lora_b_hl[:, h * HALF:(h + 1) * HALF],
                              start=False, stop=True).then_inc(half_done, 1)

            in_groups(pe, turn)

        @block.vector
        def _(dve):
            def split_x(p, s, opening):
                for b in range(2):
                    rows, other = slice(b * C, (b + 1) * C), slice((1 - b) * C, (2 - b) * C)
                    dve.wait_ge(x_high, 2 * p + b + 1)
                    dve.tensor_tensor(x_hl[other, s % 2, b, :], x_sb[rows, s, :],
                                      x_hl[rows, s % 2, b, :].bitcast(fp32), ALU.subtract).then_inc(x_low, 1)

            def split_y(p, s):
                for n in range(YB):
                    chunks = slice(n * KB, (n + 1) * KB)
                    dve.wait_ge(y_high, YB * p + n + 1)
                    dve.tensor_tensor(yl[:, s % 2, chunks, :], y_ps[n][:, :],
                                      yh[:, s % 2, chunks, :].bitcast(fp32), ALU.subtract).then_inc(y_low, 1)

            def split_w(h):
                for k in range(KC):
                    n = h * KC + k
                    cols = slice(h * HALF, (h + 1) * HALF)
                    dve.wait_ge(w_high, n + 1)
                    dve.tensor_tensor(wl[:, k, cols], out_ps[1][n % 2][:, :],
                                      wh[:, k, cols].bitcast(fp32), ALU.subtract).then_inc(w_low, 1)

            dve.wait_ge(lora_b_loaded, 16)
            for n in range(4):
                ins = dve.tensor_copy(lora_b4[:, :, n, :].rearrange("p j (e r) -> p j e r", e=E),
                                      lora_b_sb[:, :, :, :].rearrange("p e j r -> p j e r"))
            ins.then_inc(lora_b_copied, 1)
            split_x(0, 0, True)
            dve.wait_ge(cond_high, 1)
            dve.tensor_tensor(cond_hl[:, :, 1, :], cond_sb[:, :, :], cond_hl[:, :, 0, :].bitcast(fp32),
                              ALU.subtract).then_inc(cond_low, 1)
            dve.wait_ge(router_high, 1)
            dve.tensor_tensor(router_hl[:, :, 1, :], score_ps[:, 0:KC * GC].rearrange("p (k c) -> p k c", k=KC),
                              router_hl[:, :, 0, :].bitcast(fp32), ALU.subtract).then_inc(router_low, 1)
            dve.wait_ge(lora_b_high, 2)
            turned = lora_b_hl[:, :].rearrange("q (p j) -> q j p", j=OC)
            for g in (1, 3):
                rows = slice(g * ER, (g + 1) * ER)
                for n in range(2):
                    js = slice(n * OC // 2, (n + 1) * OC // 2)
                    ins = dve.tensor_tensor(turned[rows, js, :],
                                            out_ps[0][n][rows, :].rearrange("q (j p) -> q j p", p=P),
                                            turned[rows, js, :].bitcast(fp32), ALU.subtract)
                ins.then_inc(lora_b_low, 1)
            split_x(1, 1, True)
            split_y(0, 0)
            split_w(0)
            dve.wait_ge(bias_loaded, 16)
            dve.wait_ge(const_done, E)

            def route(p):
                def step(n, ins):
                    ins.then_inc(route_step, 1)
                    dve.wait_ge(route_step, ROUTE_STEPS * p + n)

                dve.wait_ge(scored, p + 1)
                step(1, dve.tensor_tensor(low_sum[:, :], score_ps[:, GC:2 * GC], bias_sb[:, :], ALU.add))
                step(2, dve.tensor_tensor(scores[:, :], score_ps[:, 0:GC], low_sum[:, :], ALU.add))
                step(3, dve.tensor_reduce(best[:, :], scores[:, 0:E], AX.X, ALU.max))
                step(4, dve.scalar_tensor_tensor(out=ranks[:, :], in0=scores[:, 0:E], scalar=best[:, 0:1],
                                                 in1=rank_w[:, :], op0=ALU.is_equal, op1=ALU.mult))
                step(5, dve.tensor_reduce(first[:, :], ranks[:, :], AX.X, ALU.max))
                step(6, dve.scalar_tensor_tensor(
                    out=z_sel[:, :].rearrange("p (e r) -> p e r", e=E),
                    in0=ranks[:, :].unsqueeze(2).to_broadcast([P, E, R]), scalar=first[:, 0:1],
                    in1=scores[:, E:GC].rearrange("p (e r) -> p e r", e=E), op0=ALU.is_equal, op1=ALU.mult))
                twice = z_sel[:, :].unsqueeze(1).to_broadcast([P, 2, ER])
                step(7, dve.tensor_copy(z_parts[:, 0:2, :].bitcast(fp32r), twice))
                dve.tensor_tensor(z_parts[:, 2:4, :], twice, z_parts[:, 0:2, :], ALU.subtract)\
                   .then_inc(route_step, 1)

            def add_x(p, s, opening):
                if not opening or p >= 2:
                    dve.wait_ge(stored[s % 2], 16 // 2 * (p - s % 2))
                for h in range(HALVES):
                    cols = slice(h * HALF, (h + 1) * HALF)
                    dve.wait_ge(half_done, HALVES * p + h + 1)
                    dve.tensor_tensor(out_sb[:, s % 2, cols], out_ps[s % 2][h][:, :], x_sb[:, s, cols],
                                      ALU.add).then_inc(half_out, 1)

            def turn(p, s, opening, closing):
                if not opening or s > 0:
                    add_x(p - 1, (s - 1) % UNROLL, opening)
                route(p)
                if opening and s == 0:
                    split_w(1)
                if not closing or s + 2 < UNROLL:
                    split_x(p + 2, (s + 2) % UNROLL, opening)
                if not closing or s + 1 < UNROLL:
                    split_y(p + 1, (s + 1) % UNROLL)

            in_groups(dve, turn)
            add_x(PAIRS - 1, UNROLL - 1, False)


_INS = ['x', 'itok_B_0_15', 'L0_cond_weights', 'L0_ffn_W_up', 'L0_ffn_gate_w', 'L0_ffn_expert_bias',
        'L0_ffn_lora_A', 'L0_ffn_lora_B']


def kernel(**inputs):
    import numpy as _np
    import concourse.bacc as _bacc
    from concourse import mybir as _mybir
    from concourse.bass_utils import run_bass_kernel_spmd as _run

    nc = _bacc.Bacc("TRN2", target_bir_lowering=False, num_devices=1)
    arrays, args = {}, []
    for name in _INS:
        a = _np.ascontiguousarray(inputs[name])
        arrays[f"in_{name}_dram"] = a
        args.append(nc.dram_tensor(f"in_{name}_dram", a.shape, _mybir.dt.from_np(a.dtype), kind="ExternalInput").ap())
    args.append(nc.dram_tensor("out_dram", inputs['x'].shape, _mybir.dt.float32, kind="ExternalOutput").ap())
    adaln_ffn_kernel(nc, *args)
    r = _run(nc, [arrays], core_ids=[0])
    return r.results[0]["out_dram"]
```

```python
import concourse.bass as bass
from concourse import mybir
from contextlib import ExitStack


def adaln_ffn_kernel(
    nc: bass.Bass,
    x: bass.AP,
    cond_index: bass.AP,
    cond_weights: bass.AP,
    w_up: bass.AP,
    gate_w: bass.AP,
    expert_bias: bass.AP,
    lora_a: bass.AP,
    lora_b: bass.AP,
    out: bass.AP,
):
    fp32 = mybir.dt.float32
    fp32r = mybir.dt.float32r
    i32 = mybir.dt.int32
    ALU = mybir.AluOpType
    ACT = mybir.ActivationFunctionType
    AX = mybir.AxisListType

    B, C, T = x.shape
    S, _, D = cond_weights.shape
    O, _ = w_up.shape
    E, R, _ = lora_a.shape
    P = 128
    PAIRS = B // 2
    KC = T // P
    OC = O // P
    ER = E * R
    GC = E + ER
    COLS = GC + O
    PARTS = 3
    EDGES = [0, 354, 708, COLS]
    BANK = 512
    UNROLL = 4
    KH = KC // 2
    ROUTE_STEPS = 7
    TURN_BANKS = 3
    TURNS = 1 + 2 * OC + 2
    assert C == D and 2 * D == P and PAIRS % UNROLL == 0 and PAIRS > 2 * UNROLL
    assert all(b - a <= BANK and a % 2 == 0 for a, b in zip(EDGES, EDGES[1:]))

    x_pairs = x.rearrange("(n b) c t -> n (b c) t", b=2)
    out_pairs = out.rearrange("(n b) c t -> n (b c) t", b=2)

    ctx = ExitStack()
    with ctx:
        def sb(name, shape, dt):
            return ctx.enter_context(nc.sbuf_tensor(name, shape, dt))

        def banks(name, n):
            return ctx.enter_context(nc.psum_tensor(name, [P, n, BANK], fp32))

        def sem(name):
            return ctx.enter_context(nc.semaphore(name))

        w_up_sb = sb("w_up_sb", [P, OC, T], fp32)
        cond_sb = sb("cond_sb", [P, S, D], fp32)
        router_sb = sb("router_sb", [GC, T], fp32)
        lora_b_sb = sb("lora_b_sb", [P, E, OC, R], fp32)
        bias_sb = sb("bias_sb", [P, GC], fp32)
        index_sb = sb("index_sb", [1, B], i32)
        wh = sb("wh", [P, KC, COLS], fp32r)
        wl = sb("wl", [P, KC, COLS], fp32r)
        cond_hl = sb("cond_hl", [P, S, 2, D], fp32r)
        lora_b4 = sb("lora_b4", [P, OC, 4, ER], fp32)
        lora_b_hl = sb("lora_b_hl", [P, O], fp32r)
        ident = sb("ident", [P, P], fp32)
        rank_w = sb("rank_w", [P, E], fp32)
        x_sb = sb("x_sb", [P, UNROLL, T], fp32)
        x_hl = sb("x_hl", [P, 2, 2, T], fp32r)
        y_small = sb("y_small", [P, 2, KH * P], fp32)
        y_sum = sb("y_sum", [P, 2, KH * P], fp32)
        yh = sb("yh", [P, 2, KC, P], fp32r)
        yl = sb("yl", [P, 2, KC, P], fp32r)
        out_sb = sb("out_sb", [P, 2, O], fp32)
        scores = sb("scores", [P, GC], fp32)
        best = sb("best", [P, 1], fp32)
        ranks = sb("ranks", [P, E], fp32)
        first = sb("first", [P, 1], fp32)
        z_sel = sb("z_sel", [P, ER], fp32)
        z_parts = sb("z_parts", [P, 4, ER], fp32)
        z_t = sb("z_t", [P, P], fp32r)

        out_ps = [banks(f"out_ps{s}", PARTS) for s in range(2)]
        y_ps = banks("y_ps", 2)
        y_halves = y_ps[:, :, :].rearrange("q n (g a d) -> q (n g) a d", a=2, d=D)

        ident_zero = sem("ident_zero")
        ident_done = sem("ident_done")
        const_done = sem("const_done")
        bias_zero = sem("bias_zero")
        cond_loaded = sem("cond_loaded")
        index_loaded = sem("index_loaded")
        router_loaded = sem("router_loaded")
        bias_loaded = sem("bias_loaded")
        lora_b_loaded = sem("lora_b_loaded")
        w_up_loaded = [sem(f"w_up_loaded{c}") for c in range(OC)]
        x_loaded = [sem(f"x_loaded{s}") for s in range(UNROLL)]
        stored = [sem(f"stored{s}") for s in range(2)]
        cond_high = sem("cond_high")
        cond_low = sem("cond_low")
        lora_b_copied = sem("lora_b_copied")
        turned = sem("turned")
        turned_high = sem("turned_high")
        turned_low = sem("turned_low")
        x_high = sem("x_high")
        x_low = sem("x_low")
        y_done = sem("y_done")
        y_small_out = sem("y_small_out")
        y_summed = sem("y_summed")
        y_high = sem("y_high")
        y_low = sem("y_low")
        scored = sem("scored")
        route_step = sem("route_step")
        z_turned = sem("z_turned")
        z_ready = sem("z_ready")
        part_done = sem("part_done")
        part_out = sem("part_out")

        block = ctx.enter_context(nc.Block())

        def in_groups(eng, work):
            for n in range(UNROLL):
                work(n, n, True, False)
            with eng.Fori(1, PAIRS // UNROLL - 1) as group:
                for n in range(UNROLL):
                    work(group * UNROLL + n, n, False, False)
            for n in range(UNROLL):
                work(PAIRS - UNROLL + n, n, False, True)

        AHEAD = [range(0, 7), range(7, 13), range(13, TURNS)]

        def turn_target(g, w):
            c, half = (g - 1) // 2, (g - 1) % 2
            return w[:, half * KH:(half + 1) * KH, GC + c * P:GC + (c + 1) * P]

        @block.sync
        def _(sp):
            sp.dma_start(x_sb[:, 0, :], x_pairs[0]).then_inc(x_loaded[0], 16)
            for c in range(OC):
                sp.dma_start(w_up_sb[:, c, :], w_up[c * P:(c + 1) * P, :]).then_inc(w_up_loaded[c], 16)
                if c == 2:
                    sp.dma_start(x_sb[:, 1, :], x_pairs[1]).then_inc(x_loaded[1], 16)
            for s in range(2, UNROLL):
                sp.dma_start(x_sb[:, s, :], x_pairs[s]).then_inc(x_loaded[s], 16)

            def turn(p, s, opening, closing):
                sp.wait_ge(part_out, PARTS * p + PARTS)
                sp.dma_start(out_pairs[p], out_sb[:, s % 2, :]).then_inc(stored[s % 2], 16)
                if not closing:
                    sp.dma_start(x_sb[:, s, :], x_pairs[p + UNROLL]).then_inc(x_loaded[s], 16)

            in_groups(sp, turn)
            for s in range(2):
                sp.wait_ge(stored[s], 16 * (PAIRS // 2))

        @block.gpsimd
        def _(pool):
            pool.memset(ident[:, :], 0.0).then_inc(ident_zero, 1)
            pool.memset(bias_sb[:, :], 0.0).then_inc(bias_zero, 1)
            pool.wait_ge(ident_zero, 1)
            pool.affine_select(out=ident[:, :], in_=ident[:, :], compare_op=ALU.not_equal, fill=1.0,
                               base=0, pattern=[[-1, P]], channel_multiplier=1).then_inc(ident_done, 1)
            for e in range(E):
                pool.memset(rank_w[:, e:e + 1], float(E - e)).then_inc(const_done, 1)

        @block.scalar
        def _(act):
            src = cond_weights.rearrange("s c d -> c s d")
            for part in range(2):
                act.dma_start(cond_sb[part * C:(part + 1) * C, :, :], src).then_inc(cond_loaded, 16)
            act.dma_start(index_sb[:, :], cond_index.rearrange("(a n) -> a n", a=1)).then_inc(index_loaded, 16)
            act.dma_start(router_sb[0:E, :], gate_w).then_inc(router_loaded, 16)
            act.dma_start(router_sb[E:GC, :], lora_a.rearrange("e r t -> (e r) t")).then_inc(router_loaded, 16)
            act.wait_ge(bias_zero, 1)
            act.dma_start(bias_sb[:, 0:E], expert_bias.rearrange("(a n) -> a n", a=1).to_broadcast([P, E]))\
               .then_inc(bias_loaded, 16)

            def split_x(p, s, opening):
                act.wait_ge(x_loaded[s], 16 // UNROLL * (p - s) + 16)
                if not opening or p >= 2:
                    act.wait_ge(y_done, 2 * p - 2)
                for b in range(2):
                    rows = slice(b * C, (b + 1) * C)
                    act.activation(x_hl[rows, s % 2, b, :], x_sb[rows, s, :], ACT.Copy).then_inc(x_high, 1)

            def split_y(p, s, half, opening):
                act.wait_ge(y_done, 2 * p + half + 1)
                act.activation(y_small[:, half, :].rearrange("q (g d) -> q g d", d=D), y_halves[:, :, 1, :],
                               ACT.Copy).then_inc(y_small_out, 1)
                if half == 0 and (not opening or p >= 2):
                    act.wait_ge(part_done, PARTS * (p - 1))
                act.wait_ge(y_summed, 2 * p + half + 1)
                act.activation(yh[:, s % 2, half * KH:(half + 1) * KH, :], y_sum[:, half, :], ACT.Copy)\
                   .then_inc(y_high, 1)

            def split_turned(part):
                for g in AHEAD[part]:
                    act.wait_ge(turned, g + 1)
                    src = out_ps[1][:, g % TURN_BANKS, :]
                    if g == 0:
                        dst, src = wh[:, :, 0:GC], src[:, 0:KC * GC]
                    elif g < 1 + 2 * OC:
                        dst = turn_target(g, wh)
                    else:
                        half = g - 1 - 2 * OC
                        dst = lora_b_hl[:, :].rearrange("q (p j) -> q j p", j=OC)[:, half * OC // 2:(half + 1) * OC // 2, :]
                        src = src.rearrange("q (j p) -> q j p", p=P)
                    act.activation(dst, src, ACT.Copy).then_inc(turned_high, 1)

            split_x(0, 0, True)
            act.wait_ge(cond_loaded, 32)
            act.activation(cond_hl[:, :, 0, :], cond_sb[:, :, :], ACT.Copy).then_inc(cond_high, 1)
            act.dma_start(lora_b_sb[:, :, :, :], lora_b.rearrange("e (p j) r -> p e j r", p=P))\
               .then_inc(lora_b_loaded, 16)
            for half in range(2):
                split_y(0, 0, half, True)
            split_turned(0)
            split_x(1, 1, True)

            def turn(p, s, opening, closing):
                begins = opening and s == 0
                if not begins and (not closing or s + 2 < UNROLL):
                    split_x(p + 2, (s + 2) % UNROLL, opening)
                for half in range(2):
                    if not closing or s + 1 < UNROLL:
                        split_y(p + 1, (s + 1) % UNROLL, half, opening)
                    if begins:
                        split_turned(1 + half)
                    if half == 0:
                        act.wait_ge(z_turned, p + 1)
                        if not opening or p >= 1:
                            act.wait_ge(part_done, PARTS * p)
                        act.activation(z_t[:, :], out_ps[s % 2][:, PARTS - 1, 0:P], ACT.Copy).then_inc(z_ready, 1)
                if begins:
                    split_x(p + 2, s + 2, opening)

            in_groups(act, turn)

        @block.tensor
        def _(pe):
            def load_index(p):
                return [pe.value_load(index_sb[0:1, bass.ds(2 * p + b, 1)], min_val=0, max_val=S - 1)
                        for b in range(2)]

            def make_y(p, s, half, opening, index):
                if half == 0:
                    pe.wait_ge(x_low, 2 * p + 2)
                if not opening or p >= 1 or half == 1:
                    pe.wait_ge(y_summed, 2 * p + half)
                for k in range(half * KH, (half + 1) * KH):
                    for b in range(2):
                        at = (k % 2) * 2 * P + b * P
                        mm = pe.matmul(y_ps[:, k % KH // 2, at:at + P], x_hl[:, s % 2, b, k * P:(k + 1) * P],
                                       cond_hl[:, index[b], :, :], start=True, stop=True)
                mm.then_inc(y_done, 1)

            def turn_weights(part):
                for g in AHEAD[part]:
                    if g >= TURN_BANKS:
                        pe.wait_ge(turned_low, g - TURN_BANKS + 1)
                    bank = out_ps[1][:, g % TURN_BANKS, :]
                    if g == 0:
                        pe.wait_ge(router_loaded, 32)
                        for k in range(KC):
                            mm = pe.transpose(bank[:, k * GC:(k + 1) * GC], router_sb[:, k * P:(k + 1) * P],
                                              ident[0:GC, 0:GC])
                    elif g < 1 + 2 * OC:
                        c, half = (g - 1) // 2, (g - 1) % 2
                        pe.wait_ge(w_up_loaded[c], 16)
                        for k in range(KH):
                            t0 = (half * KH + k) * P
                            mm = pe.transpose(bank[:, k * P:(k + 1) * P], w_up_sb[:, c, t0:t0 + P], ident[:, :])
                    else:
                        half = g - 1 - 2 * OC
                        pe.wait_ge(lora_b_copied, 4)
                        for j in range(OC // 2):
                            mm = pe.transpose(bank[:, j * P:(j + 1) * P],
                                              lora_b4[:, half * OC // 2 + j, :, :].rearrange("p n q -> p (n q)"),
                                              ident[:, :])
                    mm.then_inc(turned, 1)

            pe.wait_ge(ident_done, 1)
            pe.wait_ge(index_loaded, 16)
            pe.wait_ge(cond_low, 1)
            index = load_index(0)
            for half in range(2):
                make_y(0, 0, half, True, index)
            turn_weights(0)

            def turn(p, s, opening, closing):
                last = closing and s + 1 == UNROLL
                index = None if last else load_index(p + 1)

                def columns(part):
                    a, b = EDGES[part], EDGES[part + 1]
                    bank = out_ps[s % 2][:, part, 0:b - a]
                    if opening and p == 0:
                        pe.wait_ge(turned_low, AHEAD[part][-1] + 1)
                    elif opening and p == 1 and part == 0:
                        pe.wait_ge(turned_low, TURNS)
                    elif not opening or p >= 2:
                        pe.wait_ge(part_out, PARTS * (p - 2) + part + 1)
                    for k in range(KC):
                        for y, w in ((yh, wh), (yh, wl), (yl, wh)):
                            mm = pe.matmul(bank, y[:, s % 2, k, :], w[:, k, a:b],
                                           start=(k == 0 and y is yh and w is wh), stop=(k == KC - 1 and y is yl))
                    return mm

                pe.wait_ge(y_low, 2 * p + 2)
                columns(0).then_inc(scored, 1)
                if not last:
                    make_y(p + 1, (s + 1) % UNROLL, 0, opening, index)
                if opening and p == 0:
                    turn_weights(1)
                columns(1)
                pe.wait_ge(route_step, ROUTE_STEPS * p + ROUTE_STEPS)
                if not opening or p >= 2:
                    pe.wait_ge(part_out, PARTS * (p - 1))
                pe.transpose(out_ps[s % 2][:, PARTS - 1, 0:P], z_parts[:, :, :].rearrange("p n q -> p (n q)"),
                             ident[:, :]).then_inc(z_turned, 1)
                if not last:
                    make_y(p + 1, (s + 1) % UNROLL, 1, opening, index)
                if opening and p == 0:
                    turn_weights(2)
                pe.wait_ge(z_ready, p + 1)
                columns(2)
                for part in range(PARTS):
                    a, b = max(EDGES[part], GC), EDGES[part + 1]
                    pe.matmul(out_ps[s % 2][:, part, a - EDGES[part]:b - EDGES[part]], z_t[:, :],
                              lora_b_hl[:, a - GC:b - GC], start=False, stop=True,
                              skip_group_check=True).then_inc(part_done, 1)

            in_groups(pe, turn)

        @block.vector
        def _(dve):
            def split_x(p, s):
                for b in range(2):
                    rows, other = slice(b * C, (b + 1) * C), slice((1 - b) * C, (2 - b) * C)
                    dve.wait_ge(x_high, 2 * p + b + 1)
                    dve.tensor_tensor(x_hl[other, s % 2, b, :], x_sb[rows, s, :],
                                      x_hl[rows, s % 2, b, :].bitcast(fp32), ALU.subtract).then_inc(x_low, 1)

            def split_y(p, s, half):
                dve.wait_ge(y_small_out, 2 * p + half + 1)
                dve.tensor_tensor(y_sum[:, half, :].rearrange("q (g d) -> q g d", d=D), y_halves[:, :, 0, :],
                                  y_small[:, half, :].rearrange("q (g d) -> q g d", d=D), ALU.add)\
                   .then_inc(y_summed, 1)
                chunks = slice(half * KH, (half + 1) * KH)
                dve.wait_ge(y_high, 2 * p + half + 1)
                dve.tensor_tensor(yl[:, s % 2, chunks, :], y_sum[:, half, :].rearrange("q (k n) -> q k n", n=P),
                                  yh[:, s % 2, chunks, :].bitcast(fp32), ALU.subtract).then_inc(y_low, 1)

            def split_turned(part):
                for g in AHEAD[part]:
                    dve.wait_ge(turned_high, g + 1)
                    bank = out_ps[1][:, g % TURN_BANKS, :]
                    if g == 0:
                        dve.tensor_tensor(wl[:, :, 0:GC], bank[:, 0:KC * GC].rearrange("p (k c) -> p k c", c=GC),
                                          wh[:, :, 0:GC].bitcast(fp32), ALU.subtract).then_inc(turned_low, 1)
                    elif g < 1 + 2 * OC:
                        dve.tensor_tensor(turn_target(g, wl), bank.rearrange("p (k c) -> p k c", c=P),
                                          turn_target(g, wh).bitcast(fp32), ALU.subtract).then_inc(turned_low, 1)
                    else:
                        half = g - 1 - 2 * OC
                        for n in (1, 3):
                            rows = slice(n * ER, (n + 1) * ER)
                            dst = lora_b_hl[rows, :].rearrange("q (p j) -> q j p", j=OC)[:, half * OC // 2:(half + 1) * OC // 2, :]
                            ins = dve.tensor_tensor(dst, bank[rows, :].rearrange("q (j p) -> q j p", p=P),
                                                    dst.bitcast(fp32), ALU.subtract)
                        ins.then_inc(turned_low, 1)

            def route(p, s):
                def step(n, ins):
                    ins.then_inc(route_step, 1)
                    dve.wait_ge(route_step, ROUTE_STEPS * p + n)

                dve.wait_ge(scored, p + 1)
                step(1, dve.tensor_tensor(scores[:, :], out_ps[s % 2][:, 0, 0:GC], bias_sb[:, :], ALU.add))
                step(2, dve.tensor_reduce(best[:, :], scores[:, 0:E], AX.X, ALU.max))
                step(3, dve.scalar_tensor_tensor(out=ranks[:, :], in0=scores[:, 0:E], scalar=best[:, 0:1],
                                                 in1=rank_w[:, :], op0=ALU.is_equal, op1=ALU.mult))
                step(4, dve.tensor_reduce(first[:, :], ranks[:, :], AX.X, ALU.max))
                step(5, dve.scalar_tensor_tensor(
                    out=z_sel[:, :].rearrange("p (e r) -> p e r", e=E),
                    in0=ranks[:, :].unsqueeze(2).to_broadcast([P, E, R]), scalar=first[:, 0:1],
                    in1=scores[:, E:GC].rearrange("p (e r) -> p e r", e=E), op0=ALU.is_equal, op1=ALU.mult))
                twice = z_sel[:, :].unsqueeze(1).to_broadcast([P, 2, ER])
                step(6, dve.tensor_copy(z_parts[:, 0:2, :].bitcast(fp32r), twice))
                dve.tensor_tensor(z_parts[:, 2:4, :], twice, z_parts[:, 0:2, :], ALU.subtract)\
                   .then_inc(route_step, 1)

            def add_x(p, s, opening):
                if not opening or p >= 2:
                    dve.wait_ge(stored[s % 2], 16 // 2 * (p - s % 2))
                for part in range(PARTS):
                    a, b = max(EDGES[part], GC), EDGES[part + 1]
                    cols = slice(a - GC, b - GC)
                    dve.wait_ge(part_done, PARTS * p + part + 1)
                    dve.tensor_tensor(out_sb[:, s % 2, cols], out_ps[s % 2][:, part, a - EDGES[part]:b - EDGES[part]],
                                      x_sb[:, s, cols], ALU.add).then_inc(part_out, 1)

            split_x(0, 0)
            dve.wait_ge(cond_high, 1)
            dve.tensor_tensor(cond_hl[:, :, 1, :], cond_sb[:, :, :], cond_hl[:, :, 0, :].bitcast(fp32),
                              ALU.subtract).then_inc(cond_low, 1)
            for half in range(2):
                split_y(0, 0, half)
            split_turned(0)
            split_x(1, 1)
            dve.wait_ge(lora_b_loaded, 16)
            for n in range(4):
                dve.tensor_copy(lora_b4[:, :, n, :].rearrange("p j (e r) -> p j e r", e=E),
                                lora_b_sb[:, :, :, :].rearrange("p e j r -> p j e r")).then_inc(lora_b_copied, 1)
            dve.wait_ge(bias_loaded, 16)
            dve.wait_ge(const_done, E)

            def turn(p, s, opening, closing):
                begins = opening and s == 0
                if not begins:
                    add_x(p - 1, (s - 1) % UNROLL, opening)
                    if not closing or s + 2 < UNROLL:
                        split_x(p + 2, (s + 2) % UNROLL)
                route(p, s)
                for half in range(2):
                    if not closing or s + 1 < UNROLL:
                        split_y(p + 1, (s + 1) % UNROLL, half)
                    if begins:
                        split_turned(1 + half)
                if begins:
                    split_x(p + 2, s + 2)

            in_groups(dve, turn)
            add_x(PAIRS - 1, UNROLL - 1, False)


_INS = ['x', 'itok_B_0_15', 'L0_cond_weights', 'L0_ffn_W_up', 'L0_ffn_gate_w', 'L0_ffn_expert_bias',
        'L0_ffn_lora_A', 'L0_ffn_lora_B']


def kernel(**inputs):
    import numpy as _np
    import concourse.bacc as _bacc
    from concourse import mybir as _mybir
    from concourse.bass_utils import run_bass_kernel_spmd as _run

    nc = _bacc.Bacc("TRN2", target_bir_lowering=False, num_devices=1)
    arrays, args = {}, []
    for name in _INS:
        a = _np.ascontiguousarray(inputs[name])
        arrays[f"in_{name}_dram"] = a
        args.append(nc.dram_tensor(f"in_{name}_dram", a.shape, _mybir.dt.from_np(a.dtype), kind="ExternalInput").ap())
    args.append(nc.dram_tensor("out_dram", inputs['x'].shape, _mybir.dt.float32, kind="ExternalOutput").ap())
    adaln_ffn_kernel(nc, *args)
    r = _run(nc, [arrays], core_ids=[0])
    return r.results[0]["out_dram"]
```

```python
import concourse.bass as bass
from concourse import mybir
from contextlib import ExitStack


def adaln_ffn_kernel(
    nc: bass.Bass,
    x: bass.AP,
    cond_index: bass.AP,
    cond_weights: bass.AP,
    w_up: bass.AP,
    gate_w: bass.AP,
    expert_bias: bass.AP,
    lora_a: bass.AP,
    lora_b: bass.AP,
    out: bass.AP,
):
    fp32 = mybir.dt.float32
    fp32r = mybir.dt.float32r
    i32 = mybir.dt.int32
    ALU = mybir.AluOpType
    ACT = mybir.ActivationFunctionType
    AX = mybir.AxisListType

    B, C, T = x.shape
    S, _, D = cond_weights.shape
    O, _ = w_up.shape
    E, R, _ = lora_a.shape
    P = 128
    PAIRS = B // 2
    KC = T // P
    OC = O // P
    ER = E * R
    GC = E + ER
    COLS = GC + O
    PARTS = 3
    EDGES = [0, 354, 708, COLS]
    BANK = 512
    UNROLL = 4
    KH = KC // 2
    ROUTE_STEPS = 7
    WARM_UP = 40
    TURN_BANKS = 3
    TURNS = 1 + 2 * OC + 2
    assert C == D and 2 * D == P and PAIRS % UNROLL == 0 and PAIRS > 2 * UNROLL
    assert all(b - a <= BANK and a % 2 == 0 for a, b in zip(EDGES, EDGES[1:]))

    x_pairs = x.rearrange("(n b) c t -> n (b c) t", b=2)
    cond_rows = cond_weights.rearrange("s c d -> c s d")
    out_pairs = out.rearrange("(n b) c t -> n (b c) t", b=2)

    ctx = ExitStack()
    with ctx:
        def sb(name, shape, dt):
            return ctx.enter_context(nc.sbuf_tensor(name, shape, dt))

        def banks(name, n):
            return ctx.enter_context(nc.psum_tensor(name, [P, n, BANK], fp32))

        def sem(name):
            return ctx.enter_context(nc.semaphore(name))

        w_up_sb = sb("w_up_sb", [P, OC, T], fp32)
        cond_sb = sb("cond_sb", [P, S, D], fp32)
        router_sb = sb("router_sb", [GC, T], fp32)
        lora_b_sb = sb("lora_b_sb", [P, E, OC, R], fp32)
        bias_sb = sb("bias_sb", [P, GC], fp32)
        index_sb = sb("index_sb", [1, B], i32)
        wh = sb("wh", [P, KC, COLS], fp32r)
        wl = sb("wl", [P, KC, COLS], fp32r)
        cond_hl = sb("cond_hl", [P, S, 2, D], fp32r)
        lora_b4 = sb("lora_b4", [P, OC, 4, ER], fp32)
        lora_b_hl = sb("lora_b_hl", [P, O], fp32r)
        ident = sb("ident", [P, P], fp32)
        rank_w = sb("rank_w", [P, E], fp32)
        x_sb = sb("x_sb", [P, UNROLL, T], fp32)
        x_hl = sb("x_hl", [P, 2, 2, T], fp32r)
        y_small = sb("y_small", [P, 2, KH * P], fp32)
        y_sum = sb("y_sum", [P, 2, KH * P], fp32)
        yh = sb("yh", [P, 2, KC, P], fp32r)
        yl = sb("yl", [P, 2, KC, P], fp32r)
        out_sb = sb("out_sb", [P, 2, O], fp32)
        scores = sb("scores", [P, GC], fp32)
        best = sb("best", [P, 1], fp32)
        ranks = sb("ranks", [P, E], fp32)
        first = sb("first", [P, 1], fp32)
        z_sel = sb("z_sel", [P, ER], fp32)
        z_parts = sb("z_parts", [P, 4, ER], fp32)
        z_t = sb("z_t", [P, P], fp32r)

        out_ps = [banks(f"out_ps{s}", PARTS) for s in range(2)]
        y_ps = banks("y_ps", 2)
        y_halves = y_ps[:, :, :].rearrange("q n (g a d) -> q (n g) a d", a=2, d=D)

        ident_zero = sem("ident_zero")
        ident_done = sem("ident_done")
        const_done = sem("const_done")
        bias_zero = sem("bias_zero")
        cond_loaded = sem("cond_loaded")
        index_loaded = sem("index_loaded")
        router_loaded = sem("router_loaded")
        bias_loaded = sem("bias_loaded")
        lora_b_loaded = sem("lora_b_loaded")
        w_up_loaded = [sem(f"w_up_loaded{c}") for c in range(OC)]
        x_loaded = [sem(f"x_loaded{s}") for s in range(UNROLL)]
        stored = [sem(f"stored{s}") for s in range(2)]
        last_stored = sem("last_stored")
        cond_high = sem("cond_high")
        cond_low = sem("cond_low")
        lora_b_copied = sem("lora_b_copied")
        turned = sem("turned")
        turned_high = sem("turned_high")
        turned_low = sem("turned_low")
        x_high = sem("x_high")
        x_low = sem("x_low")
        y_done = sem("y_done")
        y_small_out = sem("y_small_out")
        y_summed = sem("y_summed")
        y_high = sem("y_high")
        y_low = sem("y_low")
        scored = sem("scored")
        route_step = sem("route_step")
        z_turned = sem("z_turned")
        z_ready = sem("z_ready")
        part_done = sem("part_done")
        part_out = sem("part_out")

        block = ctx.enter_context(nc.Block())

        def in_groups(eng, work):
            for n in range(UNROLL):
                work(n, n, True, False)
            with eng.Fori(1, PAIRS // UNROLL - 1) as group:
                for n in range(UNROLL):
                    work(group * UNROLL + n, n, False, False)
            for n in range(UNROLL):
                work(PAIRS - UNROLL + n, n, False, True)

        W_GROUPS, READY, past = [], [], 0
        for edge in EDGES[1:]:
            chunks = range(past, -(-(edge - GC) // P))
            past = chunks[-1] + 1
            READY.append([])
            for half in range(2):
                W_GROUPS += [(c, half) for c in chunks]
                READY[-1].append(1 + len(W_GROUPS))
        EARLY, AHEAD = range(0, 2), range(2, READY[0][1])
        WITHIN = [range(READY[0][1], READY[0][1] + KC), range(READY[0][1] + KC, TURNS)]

        def turn_target(g, w):
            c, half = W_GROUPS[g - 1]
            return w[:, half * KH:(half + 1) * KH, GC + c * P:GC + (c + 1) * P]

        @block.sync
        def _(sp):
            sp.dma_start(x_sb[:, 0, :], x_pairs[0]).then_inc(x_loaded[0], 16)
            sp.dma_start(cond_sb[C:2 * C, :, :], cond_rows).then_inc(cond_loaded, 16)
            sp.dma_start(index_sb[:, :], cond_index.rearrange("(a n) -> a n", a=1)).then_inc(index_loaded, 16)
            for c in range(OC):
                sp.dma_start(w_up_sb[:, c, :], w_up[c * P:(c + 1) * P, :]).then_inc(w_up_loaded[c], 16)
                if c == 2:
                    sp.dma_start(x_sb[:, 1, :], x_pairs[1]).then_inc(x_loaded[1], 16)
            for s in range(2, UNROLL):
                sp.dma_start(x_sb[:, s, :], x_pairs[s]).then_inc(x_loaded[s], 16)

            def turn(p, s, opening, closing):
                if closing and s + 1 == UNROLL:
                    for part in range(PARTS):
                        cols = slice(max(EDGES[part], GC) - GC, EDGES[part + 1] - GC)
                        sp.wait_ge(part_out, PARTS * p + part + 1)
                        sp.dma_start(out_pairs[p, :, cols], out_sb[:, s % 2, cols]).then_inc(last_stored, 16)
                    return
                sp.wait_ge(part_out, PARTS * p + PARTS)
                sp.dma_start(out_pairs[p], out_sb[:, s % 2, :]).then_inc(stored[s % 2], 16)
                if not closing:
                    sp.dma_start(x_sb[:, s, :], x_pairs[p + UNROLL]).then_inc(x_loaded[s], 16)

            in_groups(sp, turn)
            sp.wait_ge(stored[0], 16 * (PAIRS // 2))
            sp.wait_ge(stored[1], 16 * (PAIRS // 2 - 1))
            sp.wait_ge(last_stored, 16 * PARTS)

        @block.gpsimd
        def _(pool):
            pool.memset(ident[:, :], 0.0).then_inc(ident_zero, 1)
            pool.memset(bias_sb[:, :], 0.0).then_inc(bias_zero, 1)
            pool.wait_ge(ident_zero, 1)
            pool.affine_select(out=ident[:, :], in_=ident[:, :], compare_op=ALU.not_equal, fill=1.0,
                               base=0, pattern=[[-1, P]], channel_multiplier=1).then_inc(ident_done, 1)
            for e in range(E):
                pool.memset(rank_w[:, e:e + 1], float(E - e)).then_inc(const_done, 1)
            pool.dma_start(router_sb[0:E, :], gate_w).then_inc(router_loaded, 16)
            pool.dma_start(router_sb[E:GC, :], lora_a.rearrange("e r t -> (e r) t")).then_inc(router_loaded, 16)
            pool.wait_ge(bias_zero, 1)
            pool.dma_start(bias_sb[:, 0:E], expert_bias.rearrange("(a n) -> a n", a=1).to_broadcast([P, E]))\
                .then_inc(bias_loaded, 16)
            pool.dma_start(lora_b_sb[:, :, :, :], lora_b.rearrange("e (p j) r -> p e j r", p=P))\
                .then_inc(lora_b_loaded, 16)
            pool.wait_ge(lora_b_loaded, 16)
            for n in range(4):
                pool.tensor_copy(lora_b4[:, :, n, :].rearrange("p j (e r) -> p j e r", e=E),
                                 lora_b_sb[:, :, :, :].rearrange("p e j r -> p j e r")).then_inc(lora_b_copied, 1)

        @block.scalar
        def _(act):
            act.dma_start(cond_sb[0:C, :, :], cond_rows).then_inc(cond_loaded, 16)

            def split_x(p, s, opening):
                act.wait_ge(x_loaded[s], 16 // UNROLL * (p - s) + 16)
                if not opening or p >= 2:
                    act.wait_ge(y_done, 2 * p - 2)
                for b in range(2):
                    rows = slice(b * C, (b + 1) * C)
                    act.activation(x_hl[rows, s % 2, b, :], x_sb[rows, s, :], ACT.Copy).then_inc(x_high, 1)

            def move_small_y(p, half):
                act.wait_ge(y_done, 2 * p + half + 1)
                act.activation(y_small[:, half, :].rearrange("q (g d) -> q g d", d=D), y_halves[:, :, 1, :],
                               ACT.Copy).then_inc(y_small_out, 1)

            def round_y(p, s, half, opening):
                if half == 0 and (not opening or p >= 2):
                    act.wait_ge(part_done, PARTS * (p - 1))
                act.wait_ge(y_summed, 2 * p + half + 1)
                act.activation(yh[:, s % 2, half * KH:(half + 1) * KH, :], y_sum[:, half, :], ACT.Copy)\
                   .then_inc(y_high, 1)

            def split_turned(groups):
                for g in groups:
                    act.wait_ge(turned, g + 1)
                    src = out_ps[1][:, g % TURN_BANKS, :]
                    if g == 0:
                        dst, src = wh[:, :, 0:GC], src[:, 0:KC * GC]
                    elif g < 1 + 2 * OC:
                        dst = turn_target(g, wh)
                    else:
                        half = g - 1 - 2 * OC
                        dst = lora_b_hl[:, :].rearrange("q (p j) -> q j p", j=OC)[:, half * OC // 2:(half + 1) * OC // 2, :]
                        src = src.rearrange("q (j p) -> q j p", p=P)
                    act.activation(dst, src, ACT.Copy).then_inc(turned_high, 1)

            split_x(0, 0, True)
            act.wait_ge(cond_loaded, 32)
            act.activation(cond_hl[:, :, 0, :], cond_sb[:, :, :], ACT.Copy).then_inc(cond_high, 1)
            for half, groups in enumerate((EARLY, AHEAD)):
                move_small_y(0, half)
                split_turned(groups[:1])
                round_y(0, 0, half, True)
                split_turned(groups[1:])
            split_x(1, 1, True)
            split_turned(WITHIN[0])

            def turn(p, s, opening, closing):
                begins = opening and s == 0
                if not begins and (not closing or s + 2 < UNROLL):
                    split_x(p + 2, (s + 2) % UNROLL, opening)
                for half in range(2):
                    if not closing or s + 1 < UNROLL:
                        move_small_y(p + 1, half)
                        if begins and half == 0:
                            split_turned(WITHIN[1][:1])
                        round_y(p + 1, (s + 1) % UNROLL, half, opening)
                        if begins and half == 0:
                            split_turned(WITHIN[1][1:])
                    if half == 0:
                        act.wait_ge(z_turned, p + 1)
                        if not opening or p >= 1:
                            act.wait_ge(part_done, PARTS * p)
                        act.activation(z_t[:, :], out_ps[s % 2][:, PARTS - 1, 0:P], ACT.Copy).then_inc(z_ready, 1)
                if begins:
                    split_x(p + 2, s + 2, opening)

            in_groups(act, turn)

        @block.tensor
        def _(pe):
            def load_index(p):
                return [pe.value_load(index_sb[0:1, bass.ds(2 * p + b, 1)], min_val=0, max_val=S - 1)
                        for b in range(2)]

            def make_y(p, s, half, opening, index):
                if half == 0:
                    pe.wait_ge(x_low, 2 * p + 2)
                if not opening or p >= 1 or half == 1:
                    pe.wait_ge(y_summed, 2 * p + half)
                for k in range(half * KH, (half + 1) * KH):
                    for b in range(2):
                        at = (k % 2) * 2 * P + b * P
                        mm = pe.matmul(y_ps[:, k % KH // 2, at:at + P], x_hl[:, s % 2, b, k * P:(k + 1) * P],
                                       cond_hl[:, index[b], :, :], start=True, stop=True)
                mm.then_inc(y_done, 1)

            def turn_weights(groups):
                for g in groups:
                    if g >= TURN_BANKS:
                        pe.wait_ge(turned_low, g - TURN_BANKS + 1)
                    bank = out_ps[1][:, g % TURN_BANKS, :]
                    if g == 0:
                        pe.wait_ge(router_loaded, 32)
                        for k in range(KC):
                            mm = pe.transpose(bank[:, k * GC:(k + 1) * GC], router_sb[:, k * P:(k + 1) * P],
                                              ident[0:GC, 0:GC])
                    elif g < 1 + 2 * OC:
                        c, half = W_GROUPS[g - 1]
                        pe.wait_ge(w_up_loaded[c], 16)
                        for k in range(KH):
                            t0 = (half * KH + k) * P
                            mm = pe.transpose(bank[:, k * P:(k + 1) * P], w_up_sb[:, c, t0:t0 + P], ident[:, :])
                    else:
                        half = g - 1 - 2 * OC
                        pe.wait_ge(lora_b_copied, 4)
                        for j in range(OC // 2):
                            mm = pe.transpose(bank[:, j * P:(j + 1) * P],
                                              lora_b4[:, half * OC // 2 + j, :, :].rearrange("p n q -> p (n q)"),
                                              ident[:, :])
                    mm.then_inc(turned, 1)

            pe.wait_ge(ident_done, 1)
            for _ in range(WARM_UP):
                pe.transpose(y_ps[:, 0, 0:P], ident[:, :], ident[:, :])
            pe.wait_ge(index_loaded, 16)
            index = load_index(0)
            pe.wait_ge(cond_low, 1)
            make_y(0, 0, 0, True, index)
            turn_weights(EARLY)
            make_y(0, 0, 1, True, index)
            turn_weights(AHEAD)

            def turn(p, s, opening, closing):
                last = closing and s + 1 == UNROLL
                index = None if last else load_index(p + 1)

                def columns(part):
                    a, b = EDGES[part], EDGES[part + 1]
                    bank = out_ps[s % 2][:, part, 0:b - a]
                    if not opening or p >= 2:
                        pe.wait_ge(part_out, PARTS * (p - 2) + part + 1)
                    for k in range(KC):
                        if opening and p == 0 and k % KH == 0:
                            pe.wait_ge(turned_low, READY[part][k // KH])
                        for y, w in ((yh, wh), (yh, wl), (yl, wh)):
                            mm = pe.matmul(bank, y[:, s % 2, k, :], w[:, k, a:b],
                                           start=(k == 0 and y is yh and w is wh), stop=(k == KC - 1 and y is yl))
                        if opening and p == 0 and part < len(WITHIN):
                            turn_weights(WITHIN[part][k:k + 1])
                    return mm

                def add_delta(part):
                    a, b = max(EDGES[part], GC), EDGES[part + 1]
                    pe.matmul(out_ps[s % 2][:, part, a - EDGES[part]:b - EDGES[part]], z_t[:, :],
                              lora_b_hl[:, a - GC:b - GC], start=False, stop=True,
                              skip_group_check=True).then_inc(part_done, 1)

                pe.wait_ge(y_low, 2 * p + 2)
                columns(0).then_inc(scored, 1)
                if not last:
                    make_y(p + 1, (s + 1) % UNROLL, 0, opening, index)
                columns(1)
                pe.wait_ge(route_step, ROUTE_STEPS * p + ROUTE_STEPS)
                if not opening or p >= 2:
                    pe.wait_ge(part_out, PARTS * (p - 1))
                pe.transpose(out_ps[s % 2][:, PARTS - 1, 0:P], z_parts[:, :, :].rearrange("p n q -> p (n q)"),
                             ident[:, :]).then_inc(z_turned, 1)
                if not last:
                    make_y(p + 1, (s + 1) % UNROLL, 1, opening, index)
                pe.wait_ge(z_ready, p + 1)
                if opening and p == 0:
                    pe.wait_ge(turned_low, TURNS)
                add_delta(0)
                add_delta(1)
                columns(2)
                add_delta(2)

            in_groups(pe, turn)

        @block.vector
        def _(dve):
            def split_x(p, s):
                for b in range(2):
                    rows, other = slice(b * C, (b + 1) * C), slice((1 - b) * C, (2 - b) * C)
                    dve.wait_ge(x_high, 2 * p + b + 1)
                    dve.tensor_tensor(x_hl[other, s % 2, b, :], x_sb[rows, s, :],
                                      x_hl[rows, s % 2, b, :].bitcast(fp32), ALU.subtract).then_inc(x_low, 1)

            def sum_y(p, half):
                dve.wait_ge(y_small_out, 2 * p + half + 1)
                dve.tensor_tensor(y_sum[:, half, :].rearrange("q (g d) -> q g d", d=D), y_halves[:, :, 0, :],
                                  y_small[:, half, :].rearrange("q (g d) -> q g d", d=D), ALU.add)\
                   .then_inc(y_summed, 1)

            def low_y(p, s, half):
                chunks = slice(half * KH, (half + 1) * KH)
                dve.wait_ge(y_high, 2 * p + half + 1)
                dve.tensor_tensor(yl[:, s % 2, chunks, :], y_sum[:, half, :].rearrange("q (k n) -> q k n", n=P),
                                  yh[:, s % 2, chunks, :].bitcast(fp32), ALU.subtract).then_inc(y_low, 1)

            def split_turned(groups):
                for g in groups:
                    dve.wait_ge(turned_high, g + 1)
                    bank = out_ps[1][:, g % TURN_BANKS, :]
                    if g == 0:
                        dve.tensor_tensor(wl[:, :, 0:GC], bank[:, 0:KC * GC].rearrange("p (k c) -> p k c", c=GC),
                                          wh[:, :, 0:GC].bitcast(fp32), ALU.subtract).then_inc(turned_low, 1)
                    elif g < 1 + 2 * OC:
                        dve.tensor_tensor(turn_target(g, wl), bank.rearrange("p (k c) -> p k c", c=P),
                                          turn_target(g, wh).bitcast(fp32), ALU.subtract).then_inc(turned_low, 1)
                    else:
                        half = g - 1 - 2 * OC
                        rows = slice(2 * ER, 4 * ER)
                        dst = lora_b_hl[rows, :].rearrange("q (p j) -> q j p", j=OC)[:, half * OC // 2:(half + 1) * OC // 2, :]
                        dve.tensor_tensor(dst, bank[rows, :].rearrange("q (j p) -> q j p", p=P),
                                          dst.bitcast(fp32), ALU.subtract).then_inc(turned_low, 1)

            def route(p, s):
                def step(n, ins):
                    ins.then_inc(route_step, 1)
                    dve.wait_ge(route_step, ROUTE_STEPS * p + n)

                dve.wait_ge(scored, p + 1)
                step(1, dve.tensor_tensor(scores[:, :], out_ps[s % 2][:, 0, 0:GC], bias_sb[:, :], ALU.add))
                step(2, dve.tensor_reduce(best[:, :], scores[:, 0:E], AX.X, ALU.max))
                step(3, dve.scalar_tensor_tensor(out=ranks[:, :], in0=scores[:, 0:E], scalar=best[:, 0:1],
                                                 in1=rank_w[:, :], op0=ALU.is_equal, op1=ALU.mult))
                step(4, dve.tensor_reduce(first[:, :], ranks[:, :], AX.X, ALU.max))
                step(5, dve.scalar_tensor_tensor(
                    out=z_sel[:, :].rearrange("p (e r) -> p e r", e=E),
                    in0=ranks[:, :].unsqueeze(2).to_broadcast([P, E, R]), scalar=first[:, 0:1],
                    in1=scores[:, E:GC].rearrange("p (e r) -> p e r", e=E), op0=ALU.is_equal, op1=ALU.mult))
                twice = z_sel[:, :].unsqueeze(1).to_broadcast([P, 2, ER])
                step(6, dve.tensor_copy(z_parts[:, 0:4:2, :].bitcast(fp32r), twice))
                dve.tensor_tensor(z_parts[:, 1:4:2, :], twice, z_parts[:, 0:4:2, :], ALU.subtract)\
                   .then_inc(route_step, 1)

            def add_x(p, s, opening):
                if not opening or p >= 2:
                    dve.wait_ge(stored[s % 2], 16 // 2 * (p - s % 2))
                for part in range(PARTS):
                    a, b = max(EDGES[part], GC), EDGES[part + 1]
                    cols = slice(a - GC, b - GC)
                    dve.wait_ge(part_done, PARTS * p + part + 1)
                    dve.tensor_tensor(out_sb[:, s % 2, cols], out_ps[s % 2][:, part, a - EDGES[part]:b - EDGES[part]],
                                      x_sb[:, s, cols], ALU.add).then_inc(part_out, 1)

            split_x(0, 0)
            dve.wait_ge(cond_high, 1)
            dve.tensor_tensor(cond_hl[:, :, 1, :], cond_sb[:, :, :], cond_hl[:, :, 0, :].bitcast(fp32),
                              ALU.subtract).then_inc(cond_low, 1)
            for half, groups in enumerate((EARLY, AHEAD)):
                sum_y(0, half)
                split_turned(groups[:1])
                low_y(0, 0, half)
                split_turned(groups[1:])
            split_x(1, 1)
            split_turned(WITHIN[0])
            dve.wait_ge(bias_loaded, 16)
            dve.wait_ge(const_done, E)

            def turn(p, s, opening, closing):
                begins = opening and s == 0
                if not begins:
                    add_x(p - 1, (s - 1) % UNROLL, opening)
                    if not closing or s + 2 < UNROLL:
                        split_x(p + 2, (s + 2) % UNROLL)
                if begins:
                    sum_y(1, 0)
                    split_turned(WITHIN[1][:1])
                    low_y(1, 1, 0)
                    split_turned(WITHIN[1][1:2])
                    route(p, s)
                    split_turned(WITHIN[1][2:])
                    sum_y(1, 1)
                    low_y(1, 1, 1)
                    split_x(2, 2)
                    return
                route(p, s)
                if not closing or s + 1 < UNROLL:
                    for half in range(2):
                        sum_y(p + 1, half)
                        low_y(p + 1, (s + 1) % UNROLL, half)

            in_groups(dve, turn)
            add_x(PAIRS - 1, UNROLL - 1, False)


_INS = ['x', 'itok_B_0_15', 'L0_cond_weights', 'L0_ffn_W_up', 'L0_ffn_gate_w', 'L0_ffn_expert_bias',
        'L0_ffn_lora_A', 'L0_ffn_lora_B']


def kernel(**inputs):
    import numpy as _np
    import concourse.bacc as _bacc
    from concourse import mybir as _mybir
    from concourse.bass_utils import run_bass_kernel_spmd as _run

    nc = _bacc.Bacc("TRN2", target_bir_lowering=False, num_devices=1)
    arrays, args = {}, []
    for name in _INS:
        a = _np.ascontiguousarray(inputs[name])
        arrays[f"in_{name}_dram"] = a
        args.append(nc.dram_tensor(f"in_{name}_dram", a.shape, _mybir.dt.from_np(a.dtype), kind="ExternalInput").ap())
    args.append(nc.dram_tensor("out_dram", inputs['x'].shape, _mybir.dt.float32, kind="ExternalOutput").ap())
    adaln_ffn_kernel(nc, *args)
    r = _run(nc, [arrays], core_ids=[0])
    return r.results[0]["out_dram"]
```
